# Optimizing a Trainium2 kernel written in Bass

```python
import numpy as np
import jax
import jax.numpy as jnp

def _softmax(x, axis=-1):
    return jax.nn.softmax(x, axis=axis)

def _gelu(x):
    return jax.nn.gelu(x, approximate=True)

def _silu(x):
    return jax.nn.silu(x)

def _sigmoid(x):
    return jax.nn.sigmoid(x)

def _layernorm(x, axis=-1, eps=1e-05):
    m = jnp.mean(x, axis=axis, keepdims=True)
    v = jnp.var(x, axis=axis, keepdims=True)
    return (x - m) / jnp.sqrt(v + eps)

def _scatter_add(tgt, idx, src, axis=0):
    return tgt.at[idx].add(src)

def _segment_sum(src, seg, n):
    return jax.ops.segment_sum(src, seg, n)
kernel_name = 'mk_gps_d1_gnn_r32_7ec29e'

def setup_inputs(seed: int=0):
    np.random.seed(seed)
    _w = jnp.asarray

    def _rec_inputs():
        import jax
        import jax.numpy as jnp
        _gk = jax.random.key(seed)
        x = -0.0002117 + 1 * jax.random.normal(jax.random.fold_in(_gk, 1), (3125, 256), jnp.float32)
        src = jax.random.randint(jax.random.fold_in(_gk, 2), (50000,), 0, 3125, jnp.int32)
        dst = jax.random.randint(jax.random.fold_in(_gk, 3), (50000,), 0, 3125, jnp.int32)
        _o = jnp.argsort(dst, stable=True)
        src = src[_o]
        dst = dst[_o]
        return (x, src, dst)
    x, src, dst = _rec_inputs()

    def _L0_gnn_setup():
        import jax, jax.numpy as jnp
        import numpy as np
        N = 3125
        E = 50000
        IN_FEATS = 256
        OUT_FEATS = 256
        MAXK = 32

        def _maxk(x, k):
            _, idx = jax.lax.top_k(x, k)
            rows = jnp.arange(x.shape[0])[:, None]
            mask = jnp.zeros_like(x).at[rows, idx].set(1.0)
            return x * mask
        key = jax.random.key(seed)
        k1, k2, k3, k4, k5 = jax.random.split(key, 5)
        feat = jax.random.normal(k1, (N, IN_FEATS), dtype=jnp.float32)
        W_self = jax.random.normal(k2, (IN_FEATS, OUT_FEATS), dtype=jnp.float32) * (1.0 / np.sqrt(IN_FEATS))
        W_neigh = jax.random.normal(k3, (IN_FEATS, OUT_FEATS), dtype=jnp.float32) * (1.0 / np.sqrt(IN_FEATS))
        src = jax.random.randint(k4, (E,), 0, N, dtype=jnp.int64)
        dst = jax.random.randint(k5, (E,), 0, N, dtype=jnp.int64)
        return {'feat': feat, 'W_self': W_self, 'W_neigh': W_neigh, 'src': src, 'dst': dst}
    _L0_gnn_all = _L0_gnn_setup()
    _L0_gnn_in = {k: v for k, v in _L0_gnn_all.items() if k in ('W_self', 'W_neigh')}
    del _L0_gnn_all

    def _L0_mix_setup():
        import jax, jax.numpy as jnp
        import numpy as np
        EPS = 1e-05

        def _layernorm(x, weight, bias):
            mean = jnp.mean(x, axis=-1, keepdims=True)
            std = jnp.std(x, axis=-1, keepdims=True, ddof=1)
            out = (x - mean) / (std + EPS)
            return weight * out + bias
        key = jax.random.key(seed)
        B, N, C = (4, 1024, 256)
        H, hc = (8, C // 8)
        kx, = jax.random.split(key, 1)
        x = jax.random.normal(kx, (B, N, C), dtype=jnp.float32)
        return {'x': x, 'kln_weight': jnp.ones((H, 1, hc), dtype=jnp.float32), 'kln_bias': jnp.zeros((H, 1, hc), dtype=jnp.float32), 'vln_weight': jnp.ones((H, 1, hc), dtype=jnp.float32), 'vln_bias': jnp.zeros((H, 1, hc), dtype=jnp.float32)}
    _L0_mix_all = _L0_mix_setup()
    _L0_mix_in = {k: v for k, v in _L0_mix_all.items() if k in ('kln_weight', 'kln_bias', 'vln_weight', 'vln_bias')}
    del _L0_mix_all

    def _L0_ffn_setup():
        import jax, jax.numpy as jnp
        import numpy as np
        D_MODEL = 256
        N_EXPERTS = 16
        HIDDEN = 512
        SCALE = 0.02
        key = jax.random.key(seed)
        ks = jax.random.split(key, 5)
        x = jax.random.normal(ks[0], (4, 256, D_MODEL), dtype=jnp.float32)
        gate_w = jax.random.normal(ks[1], (D_MODEL, N_EXPERTS), dtype=jnp.float32) * SCALE
        gate_b = jnp.zeros((N_EXPERTS,), dtype=jnp.float32)
        w1 = jax.random.normal(ks[2], (N_EXPERTS, D_MODEL, HIDDEN), dtype=jnp.float32) * SCALE
        w2 = jax.random.normal(ks[3], (N_EXPERTS, D_MODEL, HIDDEN), dtype=jnp.float32) * SCALE
        w3 = jax.random.normal(ks[4], (N_EXPERTS, HIDDEN, D_MODEL), dtype=jnp.float32) * SCALE
        return {'x': x, 'gate_w': gate_w, 'gate_b': gate_b, 'w1': w1, 'w2': w2, 'w3': w3}
    _L0_ffn_all = _L0_ffn_setup()
    _L0_ffn_in = {k: v for k, v in _L0_ffn_all.items() if k in ('gate_w', 'gate_b', 'w1', 'w2', 'w3')}
    del _L0_ffn_all
    return {'x': x, 'src': src, 'dst': dst, 'L0_gnn_W_self': _L0_gnn_in['W_self'], 'L0_gnn_W_neigh': _L0_gnn_in['W_neigh'], 'L0_mix_kln_weight': _L0_mix_in['kln_weight'], 'L0_mix_kln_bias': _L0_mix_in['kln_bias'], 'L0_mix_vln_weight': _L0_mix_in['vln_weight'], 'L0_mix_vln_bias': _L0_mix_in['vln_bias'], 'L0_ffn_gate_w': _L0_ffn_in['gate_w'], 'L0_ffn_gate_b': _L0_ffn_in['gate_b'], 'L0_ffn_w1': _L0_ffn_in['w1'], 'L0_ffn_w2': _L0_ffn_in['w2'], 'L0_ffn_w3': _L0_ffn_in['w3']}

def reference(x, src, dst, L0_gnn_W_self, L0_gnn_W_neigh, L0_mix_kln_weight, L0_mix_kln_bias, L0_mix_vln_weight, L0_mix_vln_bias, L0_ffn_gate_w, L0_ffn_gate_b, L0_ffn_w1, L0_ffn_w2, L0_ffn_w3):
    import jax
    import jax.numpy as jnp

    def _L0_gnn_ref(feat, W_self, W_neigh, src, dst):
        import jax, jax.numpy as jnp
        import numpy as np
        N = 3125
        E = 50000
        IN_FEATS = 256
        OUT_FEATS = 256
        MAXK = 32

        def _maxk(x, k):
            _, idx = jax.lax.top_k(x, k)
            rows = jnp.arange(x.shape[0])[:, None]
            mask = jnp.zeros_like(x).at[rows, idx].set(1.0)
            return x * mask
        n = feat.shape[0]
        h_self = feat @ W_self
        h_neigh = feat @ W_neigh
        h_sparse = _maxk(h_neigh, MAXK)
        msg = h_sparse[src]
        summed = jax.ops.segment_sum(msg, dst, num_segments=n)
        deg = jax.ops.segment_sum(jnp.ones((src.shape[0],), dtype=feat.dtype), dst, num_segments=n)
        neigh = summed / jnp.maximum(deg, 1.0)[:, None]
        return h_self + neigh

    def _L0_mix_ref(x, kln_weight, kln_bias, vln_weight, vln_bias):
        import jax, jax.numpy as jnp
        import numpy as np
        EPS = 1e-05

        def _layernorm(x, weight, bias):
            mean = jnp.mean(x, axis=-1, keepdims=True)
            std = jnp.std(x, axis=-1, keepdims=True, ddof=1)
            out = (x - mean) / (std + EPS)
            return weight * out + bias
        B, N, C = x.shape
        H = kln_weight.shape[0]
        hc = C // H
        qkv = x.reshape(B, N, H, hc).transpose(0, 2, 1, 3)
        q = qkv
        k = _layernorm(qkv, kln_weight, kln_bias)
        v = _layernorm(qkv, vln_weight, vln_bias)
        kv = jnp.einsum('bhnd,bhne->bhde', k, v) / N
        out = jnp.einsum('bhnd,bhde->bhne', q, kv)
        out = out.transpose(0, 2, 1, 3).reshape(B, N, C)
        return out + x

    def _L0_ffn_ref(x, gate_w, gate_b, w1, w2, w3):
        import jax, jax.numpy as jnp
        import numpy as np
        D_MODEL = 256
        N_EXPERTS = 16
        HIDDEN = 512
        SCALE = 0.02
        n_experts = w1.shape[0]
        logits = jnp.einsum('bsd,de->bse', x, gate_w) + gate_b
        probs = jax.nn.softmax(logits, axis=-1)
        top_probs, top_idx = jax.lax.top_k(probs, 2)
        top_probs = top_probs / jnp.sum(top_probs, axis=-1, keepdims=True)
        dispatch = jnp.sum(jax.nn.one_hot(top_idx, n_experts, dtype=x.dtype) * top_probs[..., None], axis=-2)
        h1 = jnp.einsum('bsd,edh->bseh', x, w1)
        h2 = jnp.einsum('bsd,edh->bseh', x, w2)
        hidden = jax.nn.silu(h1) * h2
        expert_out = jnp.einsum('bseh,eho->bseo', hidden, w3)
        return jnp.einsum('bseo,bse->bso', expert_out, dispatch)
    xn = _layernorm(x, axis=-1)
    x = x + _L0_gnn_ref(xn, L0_gnn_W_self, L0_gnn_W_neigh, src, dst) + _L0_mix_ref(xn[None], L0_mix_kln_weight, L0_mix_kln_bias, L0_mix_vln_weight, L0_mix_vln_bias)[0]
    x = x + _L0_ffn_ref(_layernorm(x, axis=-1)[None], L0_ffn_gate_w, L0_ffn_gate_b, L0_ffn_w1, L0_ffn_w2, L0_ffn_w3)[0]
    return x

_drawn_inputs = setup_inputs


def setup_inputs(seed=0):
    import zlib

    import numpy as np

    out = dict(_drawn_inputs(seed))
    spreads = {'L0_mix_kln_weight': (1.0, 0.2),
     'L0_mix_kln_bias': (0.0, 0.506),
     'L0_mix_vln_weight': (1.0, 0.2),
     'L0_mix_vln_bias': (0.0, 0.502),
     'L0_ffn_gate_b': (0.0, 0.8)}
    factors = {'L0_ffn_gate_w': 8.0, 'L0_ffn_w1': 8.0, 'L0_ffn_w2': 8.0, 'L0_ffn_w3': 8.0}
    for name, (base, spread) in spreads.items():
        noise = np.random.default_rng([zlib.crc32(name.encode()), seed]).standard_normal(out[name].shape)
        drawn = base * np.exp(spread * noise) if base else spread * noise
        out[name] = jnp.asarray(drawn.astype(out[name].dtype))
    for name, factor in factors.items():
        out[name] = (out[name] * factor).astype(out[name].dtype)
    return out
```

```python
from contextlib import ExitStack

import concourse.bass as bass
from concourse import mybir

F32 = mybir.dt.float32
F16 = mybir.dt.float16
I32 = mybir.dt.int32
U32 = mybir.dt.uint32
ALU = mybir.AluOpType
ACT = mybir.ActivationFunctionType
AX = mybir.AxisListType.X
ds = bass.ds

P = 128
TAKEN = -3.0e38
LN_EPS = 1e-5
MIX_EPS = 1e-5
TOPK = 32
WSCALE = 32.0


def build(nc, x, src, dst, w_self, w_neigh, kln_w, kln_b, vln_w, vln_b,
          gate_w, gate_b, w1, w2, w3, out):
    N, D = x.shape
    TP = 125
    NT = N // TP
    BT = 5
    NB = NT // BT
    KC = D // P
    NEDGE = src.shape[0]
    GC = 4
    NG = NEDGE // (GC * TP)
    NH, _, HC = kln_w.shape
    NE, _, HID = w1.shape
    HK = HID // P
    MAXT = 64
    RING = 4
    WPIECE = KC * HID
    WROW = 6 * WPIECE
    assert NT * TP == N and NG * GC * TP == NEDGE and (2 * N + NE * (P - 1)) // P <= MAXT

    hs_dram = nc.dram_tensor("h_sparse_pairs", (N, 2 * D), F16, kind="Internal").ap()
    y_dram = nc.dram_tensor("y_pairs", (N, 2 * D), F16, kind="Internal").ap()
    w_dram = nc.dram_tensor("expert_weight_pairs", (NE, P, WROW), F16, kind="Internal").ap()
    o_dram = nc.dram_tensor("expert_rows", (2 * N + MAXT * P, D), F32, kind="Internal").ap()

    with ExitStack() as ctx:
        def sb(name, shape, dt):
            return ctx.enter_context(nc.sbuf_tensor(name, shape, dt))

        def sem(name):
            return ctx.enter_context(nc.semaphore(name))

        x_sb = sb("x_sb", [TP, NT, D], F32)
        XN, ACC = NT * D, NT * (D + 1)
        arena = sb("arena", [P, XN + ACC], F32)
        xn = arena[0:TP, 0:XN].rearrange("p (t d) -> p t d", t=NT)
        acc = arena[0:TP, XN:XN + ACC].rearrange("p (t d) -> p t d", t=NT)
        wring = arena[:, 0:RING * WROW // 2].bitcast(F16)
        obuf = arena[0:TP, 0:2 * BT * 2 * D].rearrange("p (b t d) -> p b t d", b=2, t=BT)

        wn = sb("wn", [P, KC, D], F32)
        wmix = sb("wmix", [P, KC, D], F32)
        gw = sb("gw", [P, KC, NE], F32)
        ident = sb("ident", [P, P], F32)
        ident16 = sb("ident16", [P, P], F16)
        earlier = sb("earlier", [P, P], F32)
        earlier16 = sb("earlier16", [P, P], F16)
        ones = sb("ones", [P, P], F32)
        ones16 = sb("ones16", [P, P], F16)
        zeros = sb("zeros", [1, 512], F32)
        headmask = sb("headmask", [P, P], F32)
        iota = sb("iota", [TP, N], F32)
        thr = sb("thr", [P, NT - 1], F32)
        iota_tok = sb("iota_tok", [TP, NT, 2], F32)
        iota_slot = sb("iota_slot", [P, MAXT], F32)
        upto = sb("upto", [TP, NE, NE], F32)
        rows = sb("rows", [1, 2 * D + NE], F32)
        rowsb = sb("rowsb", [P, 2 * D + NE], F32)
        kcol = sb("kcol", [P, 2, KC], F32)

        e_i = sb("e_i", [NG, 2, GC * TP], I32)
        rep5 = sb("rep5", [TP, BT, D], F32)
        e_f = sb("e_f", [NG, 2, GC * TP], F32)
        srcT = sb("srcT", [TP, NG, GC], F32)
        dstT = sb("dstT", [TP, NG, GC], F32)
        lohi = sb("lohi", [NG, 4], F32)
        cmp = sb("cmp", [NG, NT - 1], F32)
        tab = sb("tab", [1, 256], I32)
        now_src = sb("now_src", [TP, 2 * GC], I32)
        msg = sb("msg", [TP, 2 * GC, 2 * D + 2], F16)
        oh_dst = sb("oh_dst", [TP, GC, TP], F16)

        y5 = sb("y5", [TP, BT, D], F32)
        hsp5 = sb("hsp5", [TP, BT, D], F32)
        pair5 = sb("pair5", [TP, BT, 2 * D], F16)
        yT = sb("yT", [P, BT, KC, TP], F32)
        stats = sb("stats", [TP, BT, 6], F32)
        mv = sb("mv", [TP, BT, 2], F32)
        ve = sb("ve", [TP, BT], F32)
        sd = sb("sd", [TP, BT], F32)
        rc = sb("rc", [TP, BT], F32)
        max8 = sb("max8", [TP, BT, 8], F32)

        zc = sb("zc", [TP, NH, HC], F32)
        sq = sb("sq", [TP, NH, HC], F32)
        z = sb("z", [TP, KC, P + 1], F32)
        hm = sb("hm", [TP, NH], F32)
        hv = sb("hv", [TP, NH], F32)
        hsd = sb("hsd", [TP, NH], F32)
        hr = sb("hr", [TP, NH], F32)
        kv1 = sb("kv1", [P, P], F32)
        kv2 = sb("kv2", [P, P], F32)
        xst = sb("xst", [TP, D], F32)
        xsT = sb("xsT", [P, KC, TP], F32)
        wl = sb("wl", [P, WPIECE], F32)
        wp = sb("wp", [P, 2, WPIECE], F16)

        rdeg = sb("rdeg", [TP, NT], F32)
        lg5 = sb("lg5", [TP, BT, NE], F32)
        mi5 = sb("mi5", [TP, BT, 8], U32)
        pick = sb("pick", [TP, NT, 2], F32)
        gap = sb("gap", [TP, NT], F32)
        wk = sb("wk", [TP, NT, 2], F32)
        ohe = sb("ohe", [TP, 2, NT, NE], F32)
        mask16 = sb("mask16", [TP, NT, NE], F16)
        base = sb("base", [TP, NT, NE], F32)
        pr = sb("pr", [TP, NT, NE], F32)
        nexp = sb("nexp", [TP, NE], F32)
        gt = sb("gt", [TP, NE, NT - 1], F32)
        te = sb("te", [TP, NE], F32)
        ends = sb("ends", [TP, NE], F32)
        starts = sb("starts", [TP, NE], F32)
        slot = sb("slot", [TP, NT, 2], F32)
        slot_i = sb("slot_i", [TP, NT, 2], I32)
        sl_i = sb("sl_i", [TP, 2, NT, 2], I32)
        slot_hi = sb("slot_hi", [TP, NT, 2], F32)
        slot_lo = sb("slot_lo", [TP, NT, 2], F32)
        oh_lo = sb("oh_lo", [TP, 2 * BT, P], F32)
        oh_hi = sb("oh_hi", [TP, 2 * BT, MAXT], F32)
        oh_val = sb("oh_val", [TP, 2 * BT, 2, MAXT], F32)
        inv = sb("inv", [P, 2, MAXT], F32)
        free = sb("free", [P, MAXT], F32)
        dest = sb("dest", [P, MAXT], F32)
        tok = sb("tok", [P, MAXT], F32)
        tok_i = sb("tok_i", [P, MAXT], I32)
        tok_s = sb("tok_s", [P, MAXT], I32)
        wslot = sb("wslot", [P, MAXT], F32)
        eot = sb("eot", [1, MAXT], F32)
        ecmp = sb("ecmp", [1, MAXT, NE - 1], F32)
        tab_e = sb("tab_e", [1, MAXT], I32)
        tab_r = sb("tab_r", [1, MAXT], I32)
        tab_end = sb("tab_end", [1, NE + 2], I32)

        now_tok = sb("now_tok", [P, 2], I32)
        now_dst = sb("now_dst", [P, 2], I32)
        xg = sb("xg", [P, 2, 2 * D], F16)
        xT = sb("xT", [P, 2, 2 * KC, P], F16)
        act1 = wl[:, :].rearrange("p (b h) -> p b h", b=2)
        hid = wp[:, :, :].rearrange("p a n -> p (a n)").bitcast(F32).rearrange("p (b h) -> p b h", b=2)
        hT = sb("hT", [P, 2, 2, HID], F16)
        orow = sb("orow", [P, 2, D], F32)

        bank = [ctx.enter_context(nc.psum_tensor(f"bank{i}", [P, 512], F32)) for i in range(8)]
        ps_T = [bank[0][:, 0:KC * TP].rearrange("p (c t) -> p c t", c=KC),
                bank[1][:, 0:KC * TP].rearrange("p (c t) -> p c t", c=KC)]
        ps_h = [bank[2], bank[3]]
        ps_item = bank[4]
        ps_gram = bank[5][:, 0:KC * (P + 1)].rearrange("p (c m) -> p c m", c=KC)
        ps_srow = bank[6][:, 0:D].rearrange("p (c m) -> p c m", c=KC)
        ps_edge = bank[7]
        ps_pos = bank[4][0:TP, 0:NT * NE].rearrange("p (t e) -> p t e", t=NT)
        ps_cnt = bank[5][0:TP, 0:NE]
        ps_inv = bank[6][:, 0:2 * MAXT].rearrange("p (a s) -> p a s", a=2)
        ps_xT = [bank[0], bank[1]]
        ps_1 = [bank[2], bank[3]]
        ps_2 = [bank[4], bank[5]]
        ps_o = [bank[6], bank[7]]

        s_consts = sem("s_consts")
        s_consts2 = sem("s_consts2")
        s_small = sem("s_small")
        s_x = sem("s_x")
        s_w = sem("s_w")
        s_edges = sem("s_edges")
        s_ef = sem("s_ef")
        s_cnt = sem("s_cnt")
        s_eT = sem("s_eT")
        s_eTc = sem("s_eTc")
        s_tabp = sem("s_tabp")
        s_tab = sem("s_tab")
        s_rowp = sem("s_rowp")
        s_row = sem("s_row")
        s_var = sem("s_var")
        s_sd = sem("s_sd")
        s_y5 = sem("s_y5")
        s_y5copied = sem("s_y5copied")
        s_T = sem("s_T")
        s_Tc = sem("s_Tc")
        s_mm = sem("s_mm")
        s_h = sem("s_h")
        s_sparse = sem("s_sparse")
        s_hi = sem("s_hi")
        s_lo5 = sem("s_lo5")
        s_pairs = sem("s_pairs")
        s_idx = sem("s_idx")
        s_msg = [sem(f"s_msg{k}") for k in range(2 * GC)]
        s_grp = sem("s_grp")
        s_oh = sem("s_oh")
        s_item = sem("s_item")
        s_added = sem("s_added")
        s_zc = sem("s_zc")
        s_sq = sem("s_sq")
        s_hv = sem("s_hv")
        s_hsd = sem("s_hsd")
        s_z = sem("s_z")
        s_gram = sem("s_gram")
        s_kv = sem("s_kv")
        s_xst = sem("s_xst")
        s_xsTp = sem("s_xsTp")
        s_xsT = sem("s_xsT")
        s_mixp = sem("s_mixp")
        s_u = sem("s_u")
        s_wl = sem("s_wl")
        s_whi = sem("s_whi")
        s_wsplit = sem("s_wsplit")
        s_wst = sem("s_wst")
        s_x1 = sem("s_x1")
        s_var2 = sem("s_var2")
        s_sd2 = sem("s_sd2")
        s_y = sem("s_y")
        s_T2 = sem("s_T2")
        s_T2c = sem("s_T2c")
        s_lg = sem("s_lg")
        s_lgc = sem("s_lgc")
        s_hi2 = sem("s_hi2")
        s_lo2 = sem("s_lo2")
        s_pairs2 = sem("s_pairs2")
        s_gap = sem("s_gap")
        s_exp = sem("s_exp")
        s_mask = sem("s_mask")
        s_pos = sem("s_pos")
        s_ohhi = sem("s_ohhi")
        s_ohw = sem("s_ohw")
        s_ohv = sem("s_ohv")
        s_invp = sem("s_invp")
        s_etab = sem("s_etab")
        s_we = sem("s_we")
        s_now = sem("s_now")
        s_xg = [sem(f"s_xg{b}") for b in range(2)]
        s_xTp = sem("s_xTp")
        s_xT = sem("s_xT")
        s_h1 = sem("s_h1")
        s_h2 = sem("s_h2")
        s_silu = sem("s_silu")
        s_hid = sem("s_hid")
        s_hhi = sem("s_hhi")
        s_hlo = sem("s_hlo")
        s_C = sem("s_C")
        s_o = sem("s_o")
        s_sc = [sem(f"s_sc{b}") for b in range(2)]
        s_ol = [sem(f"s_ol{b}") for b in range(2)]
        s_fin = sem("s_fin")
        s_out = sem("s_out")

        block = ctx.enter_context(nc.Block())

        def rows_of(dram, i):
            return dram.rearrange("(b t p) d -> b p t d", t=BT, p=TP)[i]

        def rows_dyn(dram, i):
            return dram.rearrange("(b t p) d -> p b t d", t=BT, p=TP)[:, ds(i, 1), :, :].rearrange(
                "p a t d -> p (a t) d")

        def last_user(i, k):
            return BT * i + k - 1 if k >= 2 else (BT * i if k == 0 else BT * i - 1)

        SEGS = [(0, 16, True, 0), (16, 25, True, 1), (25, 32, False, 1), (32, 48, False, 2), (48, 50, False, None)]
        NIT = NG // 2
        assert SEGS[-1][1] == NIT and NIT == 2 * NT

        @block.sync
        def _(sp):
            sp.sem_inc(s_pairs, 16)
            sp.sem_inc(s_wst, 16)
            sp.sem_inc(s_pairs2, 16)
            sp.dma_start(x_sb[:, 0:BT, :], rows_of(x, 0)).then_inc(s_x, 16)
            sp.dma_start(wn[:, :, :], w_neigh.rearrange("(c p) n -> p c n", p=P)).then_inc(s_w, 16)
            sp.dma_start(e_i[:, 0, :], src.rearrange("(g e) -> g e", g=NG)).then_inc(s_edges, 16)
            sp.dma_start(e_i[:, 1, :], dst.rearrange("(g e) -> g e", g=NG)).then_inc(s_edges, 16)
            for i in range(1, NB):
                sp.wait_ge(s_x, 16 * i)
                sp.dma_start(x_sb[:, BT * i:BT * (i + 1), :], rows_of(x, i)).then_inc(s_x, 16)
            sp.dma_start(wmix[:, :, :], w_self.rearrange("(c p) n -> p c n", p=P)).then_inc(s_small, 16)
            sp.dma_start(gw[:, :, :], gate_w.rearrange("(c p) n -> p c n", p=P)).then_inc(s_small, 16)
            sp.dma_start(rows[:, 0:D], vln_w.rearrange("h a c -> a (h c)")).then_inc(s_small, 16)
            sp.dma_start(rows[:, D:2 * D], vln_b.rearrange("h a c -> a (h c)")).then_inc(s_small, 16)
            sp.dma_start(rows[:, 2 * D:], gate_b.rearrange("(a e) -> a e", a=1)).then_inc(s_small, 16)
            with nc.allow_non_contiguous_dma("512 channel weights"):
                for a, v in enumerate((kln_w, kln_b)):
                    sp.dma_start(kcol[:, a, :], v.rearrange("(c h) a d -> (h a d) c", c=KC)).then_inc(s_small, 16)
            with nc.sync.Fori(0, NB) as i:
                sp.wait_ge(s_lo5, i + 2)
                sp.dma_start(rows_dyn(hs_dram, i), pair5[:, :, :]).then_inc(s_pairs, 16)
            for lo, hi, _, m in SEGS:
                if m is None:
                    continue
                w = (w1, w2, w3)[m]
                with nc.sync.Fori(lo, hi) as it:
                    e = nc.s_assert_within(it - 16 * m, 0, NE - 1)
                    sp.wait_ge(s_wsplit, it + 1)
                    sp.dma_start(wl[:, :].rearrange("p (c n) -> p c n", c=w.shape[1] // P),
                                 w.rearrange("e (c p) n -> p e c n", p=P)[:, ds(e, 1), :, :].rearrange(
                                     "p a c n -> p (a c) n")).then_inc(s_wl, 16)
                    sp.wait_ge(s_wsplit, it + 2)
                    sp.dma_start(w_dram[ds(e, 1), :, 2 * m * WPIECE:2 * (m + 1) * WPIECE].rearrange("a p n -> (a p) n"),
                                 wp[:, :, :].rearrange("p a n -> p (a n)")).then_inc(s_wst, 16)
            with nc.sync.Fori(0, NB) as i:
                sp.wait_ge(s_lo2, i + 2)
                sp.dma_start(rows_dyn(y_dram, i), pair5[:, :, :]).then_inc(s_pairs2, 16)
            sp.wait_ge(s_wst, 16 * (3 * NE + 1))
            sp.wait_ge(s_x1, NB)
            sp.wait_ge(s_u, NT)
            for e in range(RING):
                sp.dma_start(wring[:, e * WROW:(e + 1) * WROW], w_dram[e]).then_inc(s_we, 16)
                sp.wait_ge(s_we, 16 * (e + 1))
            sp.wait_ge(s_etab, 1)
            with nc.sync.Fori(RING, NE) as e:
                done = sp.value_load(tab_end[0:1, ds(e - RING, 1)], min_val=1, max_val=MAXT)
                sp.wait_ge(s_C, done)
                sp.nop(nofuse=True)
                sp.dma_start(wring[:, ds((e % RING) * WROW, WROW)],
                             w_dram[ds(e, 1), :, :].rearrange("a p n -> (a p) n")).then_inc(s_we, 16)
                sp.wait_ge(s_we, 16 * e + 16)
                sp.nop(nofuse=True)
            last_pair = sp.value_load(tab_end[0:1, NE:NE + 1], min_val=NE // 2 - 1, max_val=MAXT // 2 - 1)
            for b in range(2):
                sp.wait_ge(s_sc[b], 16 * last_pair + 16)
            sp.wait_ge(s_C, 2 * last_pair + 2)
            o_rows = o_dram[0:2 * N, :].rearrange("(n k) d -> n (k d)", k=2)
            for i in range(NB):
                if i >= 2:
                    sp.wait_ge(s_fin, i - 1)
                sp.dma_start(obuf[:, i % 2, :, :], rows_of(o_rows, i)).then_inc(s_ol[i % 2], 16)

        @block.gpsimd
        def _(pool):
            pool.sem_inc(s_lo5, 1)
            pool.sem_inc(s_lo2, 1)
            g = nc.gpsimd
            g.memset(ident[:, :], 0.0)
            g.memset(ones[:, :], 1.0)
            g.memset(zeros[:, :], 0.0)
            g.iota(iota[:, :], [[1, N]], base=0, channel_multiplier=0, allow_small_or_imprecise_dtypes=True)
            g.iota(thr[:, :], [[1, NT - 1]], base=1, channel_multiplier=0, allow_small_or_imprecise_dtypes=True)
            g.iota(iota_tok[:, :, :], [[2 * TP, NT], [1, 2]], base=1, channel_multiplier=2,
                   allow_small_or_imprecise_dtypes=True)
            g.iota(iota_slot[:, :], [[P, MAXT]], base=2 * N + 1, channel_multiplier=1,
                   allow_small_or_imprecise_dtypes=True)
            g.memset(msg[:, :, 2 * D:2 * D + 1], 1.0)
            g.memset(z[:, :, P:P + 1], 1.0)
            pool.drain()
            g.affine_select(out=ident[:, :], in_=ident[:, :], compare_op=ALU.not_equal, fill=1.0, base=0,
                            pattern=[[-1, P]], channel_multiplier=1)
            g.affine_select(out=earlier[:, :], in_=ones[:, :], compare_op=ALU.is_gt, fill=0.0, base=0,
                            pattern=[[1, P]], channel_multiplier=-1)
            g.affine_select(out=headmask[:, :].rearrange("p (h d) -> p h d", d=HC),
                            in_=ones[:, :].rearrange("p (h d) -> p h d", d=HC),
                            compare_op=ALU.is_ge, fill=0.0, base=0, pattern=[[-HC, P // HC], [0, HC]],
                            channel_multiplier=1)
            g.affine_select(out=upto[:, :, :], in_=ones[0:TP, 0:1].unsqueeze(2).to_broadcast([TP, NE, NE]),
                            compare_op=ALU.is_ge, fill=0.0, base=0, pattern=[[1, NE], [-1, NE]],
                            channel_multiplier=0)
            pool.drain()
            g.affine_select(out=headmask[:, :].rearrange("p (h d) -> p h d", d=HC),
                            in_=headmask[:, :].rearrange("p (h d) -> p h d", d=HC),
                            compare_op=ALU.is_ge, fill=0.0, base=HC - 1, pattern=[[HC, P // HC], [0, HC]],
                            channel_multiplier=-1).then_inc(s_consts, 1)
            pool.wait_ge(s_edges, 32)
            g.tensor_copy(e_f[:, :, :], e_i[:, :, :]).then_inc(s_ef, 1)

            def keep_xn(i):
                pool.wait_ge(s_y5, BT * i + BT)
                g.tensor_copy(xn[:, ds(BT * i, BT), :], y5[:, :, :]).then_inc(s_y5copied, 1)

            def low_halves(i, full, ready, signal):
                pool.wait_ge(ready, i + 1)
                g.tensor_tensor(pair5[:, :, 0:D], full[:, :, :], pair5[:, :, D:2 * D], ALU.subtract).then_inc(signal, 1)

            keep_xn(0)
            with g.Fori(0, NB - 1) as i:
                keep_xn(i + 1)
                low_halves(i, hsp5, s_hi, s_lo5)
            low_halves(NB - 1, hsp5, s_hi, s_lo5)

            pool.wait_ge(s_pairs, 16 * (NB + 1))
            with g.Fori(0, NIT) as it:
                for q in range(2):
                    pool.wait_ge(s_idx, 2 * it + q + 1)
                    pool.nop(nofuse=True)
                    for k in range(GC * q, GC * (q + 1)):
                        g.indirect_dma_start(msg[:, k, 0:2 * D], None, hs_dram,
                                             bass.IndirectOffsetOnAxis(now_src[:, k:k + 1], 0)).then_inc(s_msg[k], 16)

            with g.Fori(0, NB) as i:
                low_halves(i, y5, s_hi2, s_lo2)

            wide = [TP, 2 * BT, MAXT]
            with g.Fori(0, NB) as i:
                pool.wait_ge(s_ohhi, i + 1)
                g.tensor_tensor(oh_val[:, :, 1, :], oh_hi[:, :, :],
                                wk[:, ds(BT * i, BT), :].rearrange("p t k -> p (t k)").unsqueeze(2).to_broadcast(wide),
                                ALU.mult).then_inc(s_ohw, 1)

            pool.wait_ge(s_etab, 1)
            pool.wait_ge(s_pairs2, 16 * (NB + 1))

            def gather(r, b):
                pool.wait_ge(s_now, 2 * r + b + 1)
                pool.nop(nofuse=True)
                g.indirect_dma_start(xg[:, b, :], None, y_dram,
                                     bass.IndirectOffsetOnAxis(now_tok[:, b:b + 1], 0)).then_inc(s_xg[b], 16)

            def scatter(r, b):
                pool.wait_ge(s_o, 2 * r + b + 3)
                pool.nop(nofuse=True)
                g.indirect_dma_start(o_dram, bass.IndirectOffsetOnAxis(now_dst[:, b:b + 1], 0),
                                     orow[:, b, :], None).then_inc(s_sc[b], 16)

            last_pair = pool.value_load(tab_end[0:1, NE:NE + 1], min_val=NE // 2 - 1, max_val=MAXT // 2 - 1)
            gather(0, 0)
            gather(0, 1)
            with g.Fori(0, last_pair) as r:
                gather(r + 1, 0)
                gather(r + 1, 1)
                scatter(r, 0)
                scatter(r, 1)
            scatter(last_pair, 0)
            scatter(last_pair, 1)

        @block.scalar
        def _(act):
            a = nc.scalar
            act.sem_inc(s_o, 2)

            def roots(i, ready, signal):
                act.wait_ge(ready, i + 1)
                a.activation(sd[:, :], ve[:, :], ACT.Sqrt).then_inc(signal, 1)

            def copy_T(i, k, ready, signal):
                act.wait_ge(ready, BT * i + k + 1)
                a.copy(yT[:, k, :, :], ps_T[k % 2]).then_inc(signal, 1)

            def high_halves(i, full, ready, stored, signal):
                act.wait_ge(ready, i + 1)
                act.wait_ge(stored, 16 * i + 16)
                a.copy(pair5[:, :, D:2 * D], full[:, :, :]).then_inc(signal, 1)

            def copy_h(i, k):
                act.wait_ge(s_mm, BT * i + k + 1)
                a.copy(acc[:, ds(BT * i + k, 1), 0:D].rearrange("p a d -> p (a d)"),
                       ps_h[k % 2][0:TP, 0:D]).then_inc(s_h, 1)

            def block_1(i):
                roots(i, s_var, s_sd)
                copy_T(i, 0, s_T, s_Tc)
                for k in range(1, BT):
                    copy_T(i, k, s_T, s_Tc)
                    copy_h(i, k - 1)
                copy_h(i, BT - 1)

            block_1(0)
            with a.Fori(0, NB - 1) as i:
                block_1(i + 1)
                high_halves(i, hsp5, s_sparse, s_pairs, s_hi)
            high_halves(NB - 1, hsp5, s_sparse, s_pairs, s_hi)
            for m, t in enumerate((srcT, dstT)):
                for k in range(GC):
                    act.wait_ge(s_eT, GC * (m + 1))
                    a.copy(t[:, :, k], ps_edge[0:TP, 128 * k:128 * k + NG] if m == 0 else
                           bank[3][0:TP, 128 * k:128 * k + NG]).then_inc(s_eTc, 1)
            act.wait_ge(s_eTc, 2 * GC)
            act.wait_ge(s_tabp, 1)
            a.copy(tab[0:1, 0:228], bank[2][0:1, 0:228]).then_inc(s_tab, 1)
            act.wait_ge(s_rowp, 2)
            a.copy(rowsb[:, 0:512], bank[0][:, :]).then_inc(s_row, 1)
            a.copy(rowsb[:, 512:], bank[1][:, 0:2 * D + NE - 512]).then_inc(s_row, 1)

            def sources(it, q):
                act.wait_ge(s_grp, 2 * it + q + 1)
                a.copy(now_src[:, GC * q:GC * (q + 1)],
                       srcT[:, ds(2 * it + q, 1), :].rearrange("p a k -> p (a k)")).then_inc(s_idx, 1)

            for lo, hi, prepare, m in SEGS:
                t0 = 0 if prepare else NT
                with a.Fori(lo - t0, hi - t0) as t:
                    it = t + t0
                    sources(it, 0)
                    if prepare:
                        act.wait_ge(s_zc, t + 1)
                        a.activation(sq[:, :, :], zc[:, :, :], ACT.Square).then_inc(s_sq, 1)
                    else:
                        act.wait_ge(s_xsTp, t + 1)
                        a.copy(xst[:, :], xn[:, ds(t, 1), :].rearrange("p a d -> p (a d)")).then_inc(s_xst, 1)
                    sources(it, 1)
                    if prepare:
                        act.wait_ge(s_hv, t + 1)
                        a.activation(hsd[:, :], hv[:, :], ACT.Sqrt).then_inc(s_hsd, 1)
                    else:
                        act.wait_ge(s_xsTp, t + 2)
                        a.copy(xsT[:, :, :], ps_T[0]).then_inc(s_xsT, 1)
                    if m is not None:
                        act.wait_ge(s_wl, 16 * it + 16)
                        act.wait_ge(s_wst, 16 * it + 16)
                        a.mul(wp[:, 0, :], wl[:, :], WSCALE).then_inc(s_whi, 1)

            with a.Fori(0, NB) as i:
                roots(i, s_var2, s_sd2)
                for k in range(BT):
                    copy_T(i, k, s_T2, s_T2c)
                act.wait_ge(s_pairs2, 16 * i + 16)
                a.copy(pair5[:, :, D:2 * D], y5[:, :, :]).then_inc(s_hi2, 1)
            act.wait_ge(s_gap, NB)
            a.activation(wk[:, :, 1], gap[:, :], ACT.Exp).then_inc(s_exp, 1)

            def index_in(r, b):
                a.copy(now_tok[:, b:b + 1], tok_s[:, ds(2 * r + b, 1)]).then_inc(s_now, 1)

            def silu(r, b):
                j = 2 * r + b
                act.wait_ge(s_h1, j + 1)
                a.activation(act1[:, b, :], ps_1[b][:, :], ACT.Silu, scale=1.0 / WSCALE).then_inc(s_silu, 1)

            def hid_high(r, b):
                act.wait_ge(s_hid, 2 * r + b + 1)
                a.copy(hT[:, b, 0, :], hid[:, b, :]).then_inc(s_hhi, 1)

            def rows_out(r, b, first=False):
                j = 2 * r + b
                if not first:
                    act.wait_ge(s_sc[b], 16 * r)
                a.copy(now_dst[:, b:b + 1], tok_i[:, ds(j, 1)])
                act.wait_ge(s_C, j + 1)
                a.activation(orow[:, b, :], ps_o[b][:, 0:D], ACT.Copy, scale=wslot[:, ds(j, 1)])
                act.drain().then_inc(s_o, 1)

            act.wait_ge(s_etab, 1)
            last_pair = act.value_load(tab_end[0:1, NE:NE + 1], min_val=NE // 2 - 1, max_val=MAXT // 2 - 1)
            index_in(0, 0)
            index_in(0, 1)
            silu(0, 0)
            hid_high(0, 0)

            def pair_of_tiles(r, first=False):
                for b in range(2):
                    act.wait_ge(s_xTp, 2 * r + b + 3)
                    index_in(r + 1, b)
                silu(r, 1)
                hid_high(r, 1)
                rows_out(r, 0, first)
                silu(r + 1, 0)
                hid_high(r + 1, 0)
                rows_out(r, 1, first)

            pair_of_tiles(0, first=True)
            with a.Fori(1, last_pair) as r:
                pair_of_tiles(r)
            silu(last_pair, 1)
            hid_high(last_pair, 1)
            rows_out(last_pair, 0)
            rows_out(last_pair, 1)
            for i in range(NB):
                act.wait_ge(s_fin, i + 1)
                act.dma_start(rows_of(out, i), x_sb[:, BT * i:BT * (i + 1), :]).then_inc(s_out, 16)
            act.wait_ge(s_out, 16 * NB)

        @block.vector
        def _(dve):
            v = nc.vector

            def normalise(i, signal_var, wait_sd, signal_y):
                dve.nop(nofuse=True)
                for k in range(BT):
                    v.bn_stats(stats[:, k, :], x_sb[:, ds(BT * i + k, 1), :].rearrange("p a d -> p (a d)"))
                dve.drain()
                for k in range(BT):
                    v.bn_aggr(mv[:, k, :], stats[:, k, :])
                dve.drain()
                v.tensor_scalar(ve[:, :], mv[:, :, 1], LN_EPS, None, ALU.add).then_inc(signal_var, 1)
                dve.wait_ge(wait_sd, i + 1)
                root_step(ve, sd, rc)
                v.reciprocal(sd[:, :], rc[:, :])
                dve.drain()
                v.tensor_scalar(rc[:, :], sd[:, :], 2.0, None, ALU.mult)
                dve.drain()
                for k in range(BT):
                    v.tensor_scalar(y5[:, k, :], x_sb[:, ds(BT * i + k, 1), :].rearrange("p a d -> p (a d)"),
                                    mv[:, k, 0:1], rc[:, k:k + 1], ALU.subtract, ALU.mult).then_inc(signal_y, 1)

            def root_step(square, root, twice):
                v.reciprocal(twice[:, :], root[:, :])
                dve.drain()
                v.tensor_tensor(twice[:, :], square[:, :], twice[:, :], ALU.mult)
                dve.drain()
                v.tensor_tensor(twice[:, :], twice[:, :], root[:, :], ALU.add)
                dve.drain()

            def sparse(i):
                dve.drain()
                dve.wait_ge(s_h, BT * i + BT)
                v.tensor_copy(rep5[:, :, :], acc[:, ds(BT * i, BT), 0:D])
                dve.drain()
                for _ in range(TOPK // 8):
                    for k in range(BT):
                        v.max(max8[:, k, :], rep5[:, k, :])
                    dve.drain()
                    for k in range(BT):
                        v.match_replace(rep5[:, k, :], max8[:, k, :], rep5[:, k, :], TAKEN)
                    dve.drain()
                dve.wait_ge(s_lo5, i + 1)
                v.scalar_tensor_tensor(hsp5[:, :, :], rep5[:, :, :], TAKEN, acc[:, ds(BT * i, BT), 0:D],
                                       ALU.is_equal, ALU.mult).then_inc(s_sparse, 1)

            dve.wait_ge(s_x, 16)
            normalise(0, s_var, s_sd, s_y5)
            dve.wait_ge(s_consts, 1)
            v.tensor_copy(ident16[:, :], ident[:, :])
            v.tensor_copy(ones16[:, :], ones[:, :])
            v.tensor_copy(earlier16[:, :], earlier[:, :]).then_inc(s_consts2, 1)
            dve.wait_ge(s_ef, 1)
            v.tensor_reduce(lohi[:, 0:1], e_f[:, 1, :], AX, ALU.min)
            v.tensor_reduce(lohi[:, 1:2], e_f[:, 1, :], AX, ALU.max)
            dve.drain()
            for a_ in range(2):
                v.tensor_scalar(cmp[:, :], thr[0:NG, :], float(TP), lohi[:, a_:a_ + 1], ALU.mult, ALU.is_le)
                dve.drain()
                v.tensor_reduce(lohi[:, 2 + a_:3 + a_], cmp[:, :], AX, ALU.add)
                dve.drain()
            v.tensor_tensor(lohi[:, 3:4], lohi[:, 3:4], lohi[:, 2:3], ALU.subtract)
            dve.drain()
            v.tensor_scalar(lohi[:, 3:4], lohi[:, 3:4], 1.0, None, ALU.add).then_inc(s_cnt, 1)

            with v.Fori(0, NB - 1) as i:
                dve.wait_ge(s_x, 16 * i + 32)
                dve.wait_ge(s_T, BT * i + BT)
                dve.wait_ge(s_y5copied, i + 1)
                normalise(i + 1, s_var, s_sd, s_y5)
                sparse(i)
            sparse(NB - 1)
            dve.drain()
            v.memset(acc[:, :, :], 0.0)

            def group(it, q):
                gi = 2 * it + q
                first = dve.value_load(tab[0:1, ds(gi, 1)], min_val=0, max_val=NG * NT)
                end = dve.value_load(tab[0:1, ds(gi + 1, 1)], min_val=1, max_val=NG * NT)
                tile0 = dve.value_load(tab[0:1, ds(gi + 128, 1)], min_val=0, max_val=NT - 1)
                with v.Fori(first, end) as item:
                    tile = nc.s_assert_within(item - first + tile0, 0, NT - 1)
                    dve.drain()
                    v.tensor_tensor(
                        oh_dst[:, :, :],
                        iota[:, ds(tile * TP, TP)].unsqueeze(1).to_broadcast([TP, GC, TP]),
                        dstT[:, ds(gi, 1), :].rearrange("p a k -> p (a k)").unsqueeze(2).to_broadcast([TP, GC, TP]),
                        ALU.is_equal).then_inc(s_oh, 1)
                    dve.wait_ge(s_item, item + 1)
                    v.tensor_tensor(acc[:, ds(tile, 1), :].rearrange("p a d -> p (a d)"), ps_item[0:TP, 0:D + 1],
                                    acc[:, ds(tile, 1), :].rearrange("p a d -> p (a d)"), ALU.add)

            def centre(t):
                heads = xn[:, ds(t, 1), :].rearrange("p a (h c) -> p (a h) c", c=HC)
                v.tensor_reduce(hm[:, :], heads, AX, ALU.add)
                dve.drain()
                v.tensor_scalar(hm[:, :], hm[:, :], 1.0 / HC, None, ALU.mult)
                dve.drain()
                v.tensor_tensor(zc[:, :, :], heads, hm[:, :].unsqueeze(2).to_broadcast([TP, NH, HC]),
                                ALU.subtract).then_inc(s_zc, 1)

            def spread(t):
                dve.wait_ge(s_sq, t + 1)
                v.tensor_reduce(hv[:, :], sq[:, :, :], AX, ALU.add)
                dve.drain()
                v.tensor_scalar(hv[:, :], hv[:, :], 1.0 / (HC - 1), 1e-30, ALU.mult, ALU.max).then_inc(s_hv, 1)

            def scale(t):
                dve.wait_ge(s_hsd, t + 1)
                root_step(hv, hsd, hr)
                v.tensor_scalar(hsd[:, :], hr[:, :], 0.5, MIX_EPS, ALU.mult, ALU.add)
                dve.drain()
                v.reciprocal(hr[:, :], hsd[:, :])
                dve.drain()
                dve.wait_ge(s_gram, t + 1)
                v.tensor_tensor(z[:, :, 0:P].rearrange("p c (h d) -> p c h d", d=HC),
                                zc[:, :, :].rearrange("p (c h) d -> p c h d", c=KC),
                                hr[:, :].rearrange("p (c h) -> p c h", c=KC).unsqueeze(3).to_broadcast(
                                    [TP, KC, NH // KC, HC]), ALU.mult).then_inc(s_z, 1)

            def finish_kv():
                dve.wait_ge(s_gram, NT + 1)
                dve.wait_ge(s_small, 7 * 16)
                dve.wait_ge(s_row, 2)
                for c in range(KC):
                    vw = rowsb[:, c * P:(c + 1) * P]
                    vb = rowsb[:, D + c * P:D + (c + 1) * P]
                    v.tensor_scalar(kv2[:, :], vb, ps_gram[:, c, P:P + 1], None, ALU.mult)
                    v.tensor_tensor(kv1[:, :], ps_gram[:, c, 0:P], vw, ALU.mult)
                    dve.drain()
                    v.tensor_tensor(kv1[:, :], kv1[:, :], kv2[:, :], ALU.add)
                    dve.drain()
                    v.tensor_scalar(kv1[:, :], kv1[:, :], kcol[:, 0, c:c + 1], None, ALU.mult)
                    v.tensor_tensor(kv2[:, :], ps_srow[:, c, :], vw, ALU.mult)
                    dve.drain()
                    v.scalar_tensor_tensor(kv2[:, :], vb, float(N), kv2[:, :], ALU.mult, ALU.add)
                    dve.drain()
                    v.scalar_tensor_tensor(kv1[:, :], kv2[:, :], kcol[:, 1, c:c + 1], kv1[:, :], ALU.mult, ALU.add)
                    dve.drain()
                    v.tensor_tensor(kv1[:, :], kv1[:, :], headmask[:, :], ALU.mult)
                    dve.drain()
                    v.scalar_tensor_tensor(kv1[:, :], kv1[:, :], 1.0 / N, ident[:, :], ALU.mult, ALU.add)
                    dve.drain()
                    v.tensor_tensor(wmix[:, c, c * P:(c + 1) * P], wmix[:, c, c * P:(c + 1) * P], kv1[:, :], ALU.add)
                    dve.drain()
                v.tensor_copy(kv2[:, 0:1], kv1[:, 0:1]).then_inc(s_kv, 1)

            def low_weights(it):
                dve.wait_ge(s_whi, it + 1)
                v.scalar_tensor_tensor(wp[:, 1, :], wl[:, :], WSCALE, wp[:, 0, :], ALU.mult,
                                       ALU.subtract).then_inc(s_wsplit, 1)

            def mixed(t):
                dve.wait_ge(s_mixp, t + 1)
                v.tensor_tensor(x_sb[:, ds(t, 1), :].rearrange("p a d -> p (a d)"), ps_h[0][0:TP, 0:D],
                                x_sb[:, ds(t, 1), :].rearrange("p a d -> p (a d)"), ALU.add).then_inc(s_u, 1)

            dve.sem_inc(s_wsplit, 1)
            dve.wait_ge(s_tab, 1)
            dve.wait_ge(s_eTc, 2 * GC)
            for lo, hi, prepare, m in SEGS:
                t0 = 0 if prepare else NT
                with v.Fori(lo - t0, hi - t0) as t:
                    it = t + t0
                    if prepare:
                        centre(t)
                    group(it, 0)
                    if prepare:
                        spread(t)
                    if m is not None:
                        low_weights(it)
                    if prepare:
                        scale(t)
                    group(it, 1)
                    if not prepare:
                        mixed(t)
                if hi == NT:
                    finish_kv()
            dve.drain()

            v.tensor_scalar(rdeg[:, :], acc[:, :, D], 1.0, None, ALU.max)
            dve.drain()
            v.reciprocal(gap[:, :], rdeg[:, :])
            dve.drain()
            v.tensor_copy(rdeg[:, :], gap[:, :])
            dve.drain()
            dve.wait_ge(s_y5copied, NB)
            with v.Fori(0, NB) as i:
                for k in range(BT):
                    row = x_sb[:, ds(BT * i + k, 1), :].rearrange("p a d -> p (a d)")
                    v.scalar_tensor_tensor(row, acc[:, ds(BT * i + k, 1), 0:D].rearrange("p a d -> p (a d)"),
                                           rdeg[:, ds(BT * i + k, 1)], row, ALU.mult, ALU.add)
                dve.drain().then_inc(s_x1, 1)
                dve.wait_ge(s_lo2, i + 1)
                normalise(i, s_var2, s_sd2, s_y)
                for k in range(BT):
                    dve.wait_ge(s_lg, BT * i + k + 1)
                    v.tensor_tensor(lg5[:, k, :], ps_h[k % 2][0:TP, 0:NE], rowsb[0:TP, 2 * D:], ALU.add).then_inc(s_lgc, 1)
                dve.drain()
                for k in range(BT):
                    v.max(max8[:, k, :], lg5[:, k, :])
                dve.drain()
                for k in range(BT):
                    v.max_index(mi5[:, k, :], max8[:, k, :], lg5[:, k, :])
                v.tensor_tensor(gap[:, ds(BT * i, BT)], max8[:, :, 1], max8[:, :, 0], ALU.subtract)
                dve.drain()
                v.tensor_copy(pick[:, ds(BT * i, BT), :], mi5[:, :, 0:2]).then_inc(s_gap, 1)
            dve.drain()

            iota_e = iota[:, 0:NE].unsqueeze(1).to_broadcast([TP, NT, NE])
            for k in range(2):
                v.tensor_tensor(ohe[:, k, :, :], iota_e, pick[:, :, k].unsqueeze(2).to_broadcast([TP, NT, NE]),
                                ALU.is_equal)
            dve.drain()
            v.tensor_tensor(mask16[:, :, :], ohe[:, 0, :, :], ohe[:, 1, :, :], ALU.add).then_inc(s_mask, 1)
            dve.wait_ge(s_exp, 1)
            v.tensor_scalar(gap[:, :], wk[:, :, 1], 1.0, None, ALU.add)
            dve.drain()
            v.reciprocal(wk[:, :, 0], gap[:, :])
            dve.drain()
            v.tensor_tensor(wk[:, :, 1], wk[:, :, 1], wk[:, :, 0], ALU.mult)
            dve.wait_ge(s_pos, 1)
            v.tensor_copy(nexp[:, :], ps_cnt)
            dve.drain()
            v.tensor_scalar(nexp[:, :], nexp[:, :], 1.0 / P, None, ALU.mult)
            dve.drain()
            v.tensor_tensor(gt[:, :, :], nexp[:, :].unsqueeze(2).to_broadcast([TP, NE, NT - 1]),
                            thr[0:TP, :].unsqueeze(1).to_broadcast([TP, NE, NT - 1]), ALU.is_gt)
            dve.drain()
            v.tensor_reduce(te[:, :], gt[:, :, :], AX, ALU.add)
            dve.drain()
            v.tensor_scalar(te[:, :], te[:, :], 1.0, None, ALU.add)
            dve.drain()
            v.tensor_tensor(pr[:, 0:NE, :], upto[:, :, :], te[:, :].unsqueeze(1).to_broadcast([TP, NE, NE]), ALU.mult)
            dve.drain()
            v.tensor_reduce(ends[:, :], pr[:, 0:NE, :], AX, ALU.add)
            dve.drain()
            v.tensor_tensor(starts[:, :], ends[:, :], te[:, :], ALU.subtract)
            dve.drain()
            v.scalar_tensor_tensor(base[:, :, :], starts[:, :].unsqueeze(1).to_broadcast([TP, NT, NE]), float(P),
                                   ps_pos, ALU.mult, ALU.add)
            dve.drain()
            for k in range(2):
                v.tensor_tensor(pr[:, :, :], ohe[:, k, :, :], base[:, :, :], ALU.mult)
                dve.drain()
                v.tensor_reduce(slot[:, :, k], pr[:, :, :], AX, ALU.add)
                dve.drain()
            v.tensor_copy(slot_i[:, :, :], slot[:, :, :])
            dve.drain()
            v.tensor_scalar(sl_i[:, 0, :, :], slot_i[:, :, :], 7, None, ALU.arith_shift_right)
            v.tensor_scalar(sl_i[:, 1, :, :], slot_i[:, :, :], P - 1, None, ALU.bitwise_and)
            dve.drain()
            v.tensor_copy(slot_hi[:, :, :], sl_i[:, 0, :, :])
            v.tensor_copy(slot_lo[:, :, :], sl_i[:, 1, :, :])
            dve.drain()
            with v.Fori(0, NB) as i:
                dve.wait_ge(s_invp, i + 1)

                def spread_out(a):
                    return a[:, ds(BT * i, BT), :].rearrange("p t k -> p (t k)").unsqueeze(2)

                v.tensor_tensor(oh_hi[:, :, :], iota[:, 0:MAXT].unsqueeze(1).to_broadcast([TP, 2 * BT, MAXT]),
                                spread_out(slot_hi).to_broadcast([TP, 2 * BT, MAXT]), ALU.is_equal).then_inc(s_ohhi, 1)
                v.tensor_tensor(oh_lo[:, :, :], iota[:, 0:P].unsqueeze(1).to_broadcast([TP, 2 * BT, P]),
                                spread_out(slot_lo).to_broadcast([TP, 2 * BT, P]), ALU.is_equal)
                dve.drain()
                v.tensor_tensor(oh_val[:, :, 0, :], oh_hi[:, :, :],
                                spread_out(iota_tok).to_broadcast([TP, 2 * BT, MAXT]), ALU.mult)
                dve.drain().then_inc(s_ohv, 1)
            v.tensor_tensor(ecmp[:, :, :], ends[0:1, 0:NE - 1].unsqueeze(1).to_broadcast([1, MAXT, NE - 1]),
                            iota[0:1, 0:MAXT].unsqueeze(2).to_broadcast([1, MAXT, NE - 1]), ALU.is_le)
            dve.drain()
            v.tensor_reduce(eot[:, :], ecmp[:, :, :], AX, ALU.add)
            v.tensor_copy(tab_end[0:1, 0:NE], ends[0:1, :])
            v.tensor_scalar(te[0:1, 0:1], ends[0:1, NE - 1:NE], -1.0, None, ALU.add)
            dve.drain()
            v.tensor_copy(tab_end[0:1, NE + 1:NE + 2], te[0:1, 0:1])
            v.tensor_copy(tab_e[:, :], eot[:, :])
            dve.drain()
            v.tensor_scalar(tab_end[0:1, NE:NE + 1], tab_end[0:1, NE + 1:NE + 2], 1, None, ALU.arith_shift_right)
            v.tensor_scalar(tab_r[:, :], tab_e[:, :], RING - 1, None, ALU.bitwise_and)
            dve.wait_ge(s_invp, NB + 1)
            v.tensor_copy(inv[:, :, :], ps_inv)
            dve.drain()
            v.tensor_scalar(free[:, :], inv[:, 0, :], 0.0, None, ALU.is_equal)
            v.tensor_scalar(tok[:, :], inv[:, 0, :], -1.0, 0.0, ALU.add, ALU.max)
            v.tensor_scalar(wslot[:, :], inv[:, 1, :], 1.0 / WSCALE, None, ALU.mult)
            dve.drain()
            v.tensor_tensor(free[:, :], free[:, :], iota_slot[:, :], ALU.mult)
            v.tensor_copy(tok_i[:, :], tok[:, :])
            dve.drain()
            v.scalar_tensor_tensor(dest[:, :], inv[:, 0, :], -1.0, free[:, :], ALU.add, ALU.add)
            v.tensor_scalar(tok_s[:, :], tok_i[:, :], 1, None, ALU.arith_shift_right)
            dve.drain()
            v.tensor_copy(tok_i[:, :], dest[:, :])
            dve.drain().then_inc(s_etab, 1)

            def rows_T(r, b):
                dve.wait_ge(s_xTp, 2 * r + b + 3)
                v.tensor_copy(xT[:, b, :, :], ps_xT[b][:, 0:2 * P].bitcast(F16).rearrange(
                    "p (a m) -> p a m", a=2 * KC)).then_inc(s_xT, 1)

            def gated(r, b):
                j = 2 * r + b
                dve.wait_ge(s_h2, j + 1)
                dve.wait_ge(s_silu, j + 1)
                v.scalar_tensor_tensor(hid[:, b, :], ps_2[b][:, :], 1.0 / WSCALE, act1[:, b, :], ALU.mult,
                                       ALU.mult).then_inc(s_hid, 1)

            def hid_low(r, b):
                dve.wait_ge(s_hhi, 2 * r + b + 1)
                v.tensor_tensor(hT[:, b, 1, :], hid[:, b, :], hT[:, b, 0, :], ALU.subtract).then_inc(s_hlo, 1)

            dve.wait_ge(s_etab, 1)
            last_pair = dve.value_load(tab_end[0:1, NE:NE + 1], min_val=NE // 2 - 1, max_val=MAXT // 2 - 1)
            rows_T(0, 0)
            gated(0, 0)
            hid_low(0, 0)
            rows_T(0, 1)
            with v.Fori(0, last_pair) as r:
                gated(r, 1)
                hid_low(r, 1)
                rows_T(r + 1, 0)
                gated(r + 1, 0)
                hid_low(r + 1, 0)
                rows_T(r + 1, 1)
            gated(last_pair, 1)
            hid_low(last_pair, 1)

            for i in range(NB):
                dve.wait_ge(s_ol[i % 2], 16 * (i // 2 + 1))
                for k in range(2):
                    last = v.tensor_tensor(x_sb[:, BT * i:BT * (i + 1), :], x_sb[:, BT * i:BT * (i + 1), :],
                                           obuf[:, i % 2, :, k * D:(k + 1) * D], ALU.add)
                    if k == 0:
                        dve.drain()
                last.then_inc(s_fin, 1)

        @block.tensor
        def _(pe):
            t_ = nc.tensor
            pe.sem_inc(s_grp, 2)
            pe.sem_inc(s_invp, 1)
            pe.sem_inc(s_xTp, 2)
            pe.wait_ge(s_consts2, 1)

            def turn(i, k, ready, copied):
                pe.wait_ge(ready, BT * i + k + 1)
                for c in range(KC):
                    mm = t_.transpose(ps_T[k % 2][:, c, :], y5[:, k, c * P:(c + 1) * P], ident[0:TP, 0:TP])
                return mm

            def tile_product(i, k, w, width, copied):
                pe.wait_ge(copied, BT * i + k + 1)
                for c in range(KC):
                    mm = t_.matmul(ps_h[k % 2][0:TP, 0:width], yT[:, k, c, :], w[:, c, :],
                                   start=(c == 0), stop=(c == KC - 1))
                return mm

            def block_products(i, y_ready, T, Tc, w, width, done, taken):
                for k in range(BT + 1):
                    if k < BT:
                        if k >= 2:
                            pe.wait_ge(Tc, BT * i + k - 1)
                        turn(i, k, y_ready, Tc).then_inc(T, 1)
                    if k >= 1:
                        if k >= 3:
                            pe.wait_ge(taken, BT * i + k - 2)
                        tile_product(i, k - 1, w, width, Tc).then_inc(done, 1)

            pe.wait_ge(s_w, 16)
            block_products(0, s_y5, s_T, s_Tc, wn, D, s_mm, s_h)
            with t_.Fori(1, NB) as i:
                pe.wait_ge(s_h, BT * i)
                block_products(i, s_y5, s_T, s_Tc, wn, D, s_mm, s_h)
            pe.wait_ge(s_ef, 1)
            pe.wait_ge(s_h, NT)
            for m in range(2):
                for k in range(GC):
                    t_.transpose((ps_edge if m == 0 else bank[3])[0:TP, 128 * k:128 * k + NG],
                                 e_f[:, m, k * TP:(k + 1) * TP], ident[0:NG, 0:NG]).then_inc(s_eT, 1)
            pe.wait_ge(s_cnt, 1)
            t_.matmul(bank[2][0:1, 0:128], lohi[:, 3:4], earlier[0:NG, :], start=True, stop=True)
            t_.matmul(bank[2][0:1, 128:228], lohi[:, 2:3], ident[0:NG, 0:NG], start=True, stop=True).then_inc(s_tabp, 1)
            pe.wait_ge(s_small, 7 * 16)
            t_.matmul(bank[0][:, :], ones[0:1, :], rows[:, 0:512], start=True, stop=True).then_inc(s_rowp, 1)
            t_.matmul(bank[1][:, 0:2 * D + NE - 512], ones[0:1, :], rows[:, 512:], start=True, stop=True).then_inc(s_rowp, 1)
            t_.matmul(ps_gram.rearrange("p c m -> p (c m)"), ones[0:1, :], zeros[:, 0:KC * (P + 1)], start=True,
                      stop=True, skip_group_check=True)
            t_.matmul(ps_srow.rearrange("p c m -> p (c m)"), ones[0:1, :], zeros[:, 0:D], start=True, stop=True,
                      skip_group_check=True).then_inc(s_gram, 1)

            def group(it, q):
                gi = 2 * it + q
                first = pe.value_load(tab[0:1, ds(gi, 1)], min_val=0, max_val=NG * NT)
                end = pe.value_load(tab[0:1, ds(gi + 1, 1)], min_val=1, max_val=NG * NT)
                for k in range(GC * q, GC * (q + 1)):
                    pe.wait_ge(s_msg[k], 16 * it + 16)
                pe.nop(nofuse=True)
                with t_.Fori(first, end) as item:
                    pe.wait_ge(s_oh, item + 1)
                    for k in range(GC):
                        row = msg[:, GC * q + k, :]
                        t_.matmul(ps_item[0:TP, 0:D + 1], oh_dst[:, k, :], row[:, D:2 * D + 1],
                                  start=(k == 0), stop=False, skip_group_check=True)
                        mm = t_.matmul(ps_item[0:TP, 0:D], oh_dst[:, k, :], row[:, 0:D],
                                       start=False, stop=(k == GC - 1), skip_group_check=True)
                    mm.then_inc(s_item, 1)
                pe.drain().then_inc(s_grp, 1)

            pe.wait_ge(s_tab, 1)
            for lo, hi, prepare, _ in SEGS:
                if lo == NT:
                    pe.wait_ge(s_kv, 1)
                    pe.wait_ge(s_row, 2)
                    pe.sem_inc(s_xsTp, 1)
                t0 = 0 if prepare else NT
                with t_.Fori(lo - t0, hi - t0) as t:
                    it = t + t0
                    group(it, 0)
                    if prepare:
                        pe.wait_ge(s_z, t + 1)
                        for c in range(KC):
                            t_.matmul(ps_gram[:, c, :], z[:, c, 0:P], z[:, c, :], start=False, stop=True,
                                      skip_group_check=True)
                        t_.matmul(ps_srow, ones[0:TP, :], z[:, :, 0:P], start=False, stop=True,
                                  skip_group_check=True).then_inc(s_gram, 1)
                    else:
                        pe.wait_ge(s_xst, t + 1)
                        for c in range(KC):
                            mm = t_.transpose(ps_T[0][:, c, :], xst[:, c * P:(c + 1) * P], ident[0:TP, 0:TP])
                        mm.then_inc(s_xsTp, 1)
                    group(it, 1)
                    if not prepare:
                        pe.wait_ge(s_xsT, t + 1)
                        for c in range(KC):
                            mm = t_.matmul(ps_h[0][0:TP, 0:D], xsT[:, c, :], wmix[:, c, :], start=(c == 0),
                                           stop=(c == KC - 1))
                        mm.then_inc(s_mixp, 1)

            block_products(0, s_y, s_T2, s_T2c, gw, NE, s_lg, s_lgc)
            with t_.Fori(1, NB) as i:
                pe.wait_ge(s_lgc, BT * i)
                block_products(i, s_y, s_T2, s_T2c, gw, NE, s_lg, s_lgc)
            pe.wait_ge(s_mask, 1)
            flat = ps_pos.rearrange("p t e -> p (t e)")
            t_.matmul(flat, earlier16[0:TP, 0:TP], mask16[:, :, :].rearrange("p t e -> p (t e)"), start=True,
                      stop=False, skip_group_check=True)
            for t in range(NT - 1):
                t_.matmul(ps_pos[:, t + 1:NT, :], ones16[0:TP, 0:TP],
                          mask16[:, t:t + 1, :].to_broadcast([TP, NT - 1 - t, NE]), start=False, stop=(t == NT - 2),
                          skip_group_check=True)
            for t in range(NT):
                mm = t_.matmul(ps_cnt, ones16[0:TP, 0:TP], mask16[:, t, :], start=(t == 0), stop=(t == NT - 1))
            mm.then_inc(s_pos, 1)
            t_.matmul(bank[6][:, 0:2 * MAXT], ones[0:1, :], zeros[:, 0:2 * MAXT], start=True, stop=True,
                      skip_group_check=True)
            with t_.Fori(0, NB) as i:
                pe.wait_ge(s_ohv, i + 1)
                pe.wait_ge(s_ohw, i + 1)
                for n in range(2 * BT):
                    mm = t_.matmul(bank[6][:, 0:2 * MAXT], oh_lo[:, n, :],
                                   oh_val[:, n, :, :].rearrange("p a s -> p (a s)"), start=False, stop=True,
                                   skip_group_check=True)
                mm.then_inc(s_invp, 1)

            pe.wait_ge(s_etab, 1)

            def turn_rows(r, b):
                pe.wait_ge(s_xg[b], 16 * r + 16)
                view = ps_xT[b][:, 0:2 * P].bitcast(F16).rearrange("p (a m) -> p a m", a=2 * KC)
                for n in range(2 * KC):
                    mm = t_.transpose(view[:, n, :], xg[:, b, n * P:(n + 1) * P], ident16[:, :])
                mm.then_inc(s_xTp, 1)

            def ring_of(j):
                return pe.value_load(tab_r[0:1, ds(j, 1)], min_val=0, max_val=RING - 1)

            def up(r, b):
                j = 2 * r + b
                e = pe.value_load(tab_e[0:1, ds(j, 1)], min_val=0, max_val=NE - 1)
                off = ring_of(j) * WROW
                pe.wait_ge(s_we, 16 * e + 16)
                pe.wait_ge(s_xT, j + 1)
                for n, (ps, done) in enumerate(((ps_1[b], s_h1), (ps_2[b], s_h2))):
                    for h in range(HK):
                        first = True
                        for c in range(KC):
                            for wpart, xpart in ((0, 1), (0, 0), (1, 1)):
                                at = (2 * n + wpart) * WPIECE + c * HID + h * P
                                mm = t_.matmul(ps[:, h * P:(h + 1) * P], wring[:, ds(off + at, P)],
                                               xT[:, b, KC * xpart + c, :], start=first,
                                               stop=(c == KC - 1 and wpart == 1))
                                first = False
                    mm.then_inc(done, 1)

            def down(r, b):
                j = 2 * r + b
                off = ring_of(j) * WROW
                pe.wait_ge(s_hlo, j + 1)
                pe.wait_ge(s_o, j + 1)
                first = True
                for h in range(HK):
                    for hpart, wpart in ((0, 0), (0, 1), (1, 0)):
                        at = (4 + wpart) * WPIECE + h * D
                        mm = t_.matmul(ps_o[b][:, 0:D], hT[:, b, hpart, h * P:(h + 1) * P], wring[:, ds(off + at, D)],
                                       start=first, stop=(h == HK - 1 and hpart == 1))
                        first = False
                mm.then_inc(s_C, 1)

            last_pair = pe.value_load(tab_end[0:1, NE:NE + 1], min_val=NE // 2 - 1, max_val=MAXT // 2 - 1)
            turn_rows(0, 0)
            up(0, 0)
            turn_rows(0, 1)
            with t_.Fori(0, last_pair) as r:
                up(r, 1)
                down(r, 0)
                turn_rows(r + 1, 0)
                up(r + 1, 0)
                down(r, 1)
                turn_rows(r + 1, 1)
            up(last_pair, 1)
            down(last_pair, 0)
            down(last_pair, 1)


_INS = ['x', 'src', 'dst', 'L0_gnn_W_self', 'L0_gnn_W_neigh', 'L0_mix_kln_weight', 'L0_mix_kln_bias',
        'L0_mix_vln_weight', 'L0_mix_vln_bias', 'L0_ffn_gate_w', 'L0_ffn_gate_b', 'L0_ffn_w1', 'L0_ffn_w2',
        'L0_ffn_w3']
_OUTS = [((3125, 256), 'float32')]


def kernel(**inputs):
    import numpy as _np
    import concourse.bacc as _bacc
    from concourse import mybir as _mybir
    from concourse.bass_utils import run_bass_kernel_spmd as _run

    nc = _bacc.Bacc("TRN2", target_bir_lowering=False, num_devices=1)
    arrays, args = {}, []
    for name in _INS:
        a = _np.ascontiguousarray(inputs[name])
        arrays[f"in_{name}_dram"] = a
        args.append(nc.dram_tensor(f"in_{name}_dram", a.shape, _mybir.dt.from_np(a.dtype), kind="ExternalInput").ap())
    for i, (shape, dtype) in enumerate(_OUTS):
        dt = _mybir.dt.from_np(_np.dtype(dtype))
        args.append(nc.dram_tensor(f"out_{i}_dram", shape, dt, kind="ExternalOutput").ap())
    build(nc, *args)
    r = _run(nc, [arrays], core_ids=[0])
    got = tuple(r.results[0][f"out_{i}_dram"] for i in range(len(_OUTS)))
    return got[0]
```
